# Optimizing a Trainium2 kernel written in Bass

```python
import numpy as np
import jax
import jax.numpy as jnp

def _softmax(x, axis=-1):
    return jax.nn.softmax(x, axis=axis)

def _gelu(x):
    return jax.nn.gelu(x, approximate=True)

def _silu(x):
    return jax.nn.silu(x)

def _sigmoid(x):
    return jax.nn.sigmoid(x)

def _layernorm(x, axis=-1, eps=1e-05):
    m = jnp.mean(x, axis=axis, keepdims=True)
    v = jnp.var(x, axis=axis, keepdims=True)
    return (x - m) / jnp.sqrt(v + eps)

def _scatter_add(tgt, idx, src, axis=0):
    return tgt.at[idx].add(src)

def _segment_sum(src, seg, n):
    return jax.ops.segment_sum(src, seg, n)
kernel_name = 'mk_adj_resnorm_d1_adj_r2_7d141e'

def setup_inputs(seed: int=0):
    np.random.seed(seed)
    _w = jnp.asarray

    def _rec_inputs():
        import jax
        import jax.numpy as jnp
        _gk = jax.random.key(seed)
        x = -0.0001538 + 1 * jax.random.normal(jax.random.fold_in(_gk, 1), (128, 128, 384), jnp.float32)
        _a = jax.random.bernoulli(jax.random.fold_in(_gk, 2), 0.125, (128, 128, 128))
        _a = jnp.logical_or(_a, jnp.swapaxes(_a, -1, -2))
        _a = jnp.logical_or(_a, jnp.eye(128, dtype=bool))
        adj = _a
        return (x, adj)
    x, adj = _rec_inputs()

    def _L0_gnn_setup():
        import jax, jax.numpy as jnp
        import numpy as np
        B, S, H = (4, 1024, 384)
        NUM_HEADS = 6
        HEAD_SIZE = H // NUM_HEADS
        NEG = -9000000000000000.0

        def _heads(x):
            b, s, _ = x.shape
            return x.reshape(b, s, NUM_HEADS, HEAD_SIZE).transpose(0, 2, 1, 3)
        key = jax.random.key(seed)
        ks = jax.random.split(key, 10)
        seq_inputs = jax.random.normal(ks[0], (B, S, H), dtype=jnp.float32)
        gm = jax.random.randint(ks[1], (B, S, S), 0, 2) > 0
        graph_mask = gm | jnp.eye(S, dtype=bool)[None]
        sc = 1.0 / np.sqrt(H)
        Wq = jax.random.normal(ks[2], (H, H), dtype=jnp.float32) * sc
        bq = jnp.zeros((H,), dtype=jnp.float32)
        Wk = jax.random.normal(ks[3], (H, H), dtype=jnp.float32) * sc
        bk = jnp.zeros((H,), dtype=jnp.float32)
        Wv = jax.random.normal(ks[4], (H, H), dtype=jnp.float32) * sc
        bv = jnp.zeros((H,), dtype=jnp.float32)
        Wf = jax.random.normal(ks[5], (H, H), dtype=jnp.float32) * sc
        bf = jnp.zeros((H,), dtype=jnp.float32)
        return {'seq_inputs': seq_inputs, 'Wq': Wq, 'bq': bq, 'Wk': Wk, 'bk': bk, 'Wv': Wv, 'bv': bv, 'Wf': Wf, 'bf': bf, 'graph_mask': graph_mask}
    _L0_gnn_all = _L0_gnn_setup()
    _L0_gnn_in = {k: v for k, v in _L0_gnn_all.items() if k in ('Wq', 'bq', 'Wk', 'bk', 'Wv', 'bv', 'Wf', 'bf')}
    del _L0_gnn_all
    return {'x': x, 'adj': adj, 'L0_gnn_Wq': _L0_gnn_in['Wq'], 'L0_gnn_bq': _L0_gnn_in['bq'], 'L0_gnn_Wk': _L0_gnn_in['Wk'], 'L0_gnn_bk': _L0_gnn_in['bk'], 'L0_gnn_Wv': _L0_gnn_in['Wv'], 'L0_gnn_bv': _L0_gnn_in['bv'], 'L0_gnn_Wf': _L0_gnn_in['Wf'], 'L0_gnn_bf': _L0_gnn_in['bf']}

def reference(x, adj, L0_gnn_Wq, L0_gnn_bq, L0_gnn_Wk, L0_gnn_bk, L0_gnn_Wv, L0_gnn_bv, L0_gnn_Wf, L0_gnn_bf):
    import jax
    import jax.numpy as jnp

    def _L0_gnn_ref(seq_inputs, Wq, bq, Wk, bk, Wv, bv, Wf, bf, graph_mask):
        import jax, jax.numpy as jnp
        import numpy as np
        B, S, H = (4, 1024, 384)
        NUM_HEADS = 6
        HEAD_SIZE = H // NUM_HEADS
        NEG = -9000000000000000.0

        def _heads(x):
            b, s, _ = x.shape
            return x.reshape(b, s, NUM_HEADS, HEAD_SIZE).transpose(0, 2, 1, 3)
        q = _heads(seq_inputs @ Wq + bq)
        k = _heads(seq_inputs @ Wk + bk)
        v = _heads(seq_inputs @ Wv + bv)
        scores = jnp.einsum('bhqd,bhkd->bhqk', q, k) / np.sqrt(HEAD_SIZE)
        bias = jnp.where(graph_mask, 0.0, NEG)[:, None]
        probs = jax.nn.softmax(scores + bias, axis=-1)
        ctx = jnp.einsum('bhqk,bhkd->bhqd', probs, v)
        ctx = ctx.transpose(0, 2, 1, 3).reshape(seq_inputs.shape[0], seq_inputs.shape[1], H)
        return ctx @ Wf + bf
    x = _layernorm(x + _L0_gnn_ref(x, L0_gnn_Wq, L0_gnn_bq, L0_gnn_Wk, L0_gnn_bk, L0_gnn_Wv, L0_gnn_bv, L0_gnn_Wf, L0_gnn_bf, adj), axis=-1)
    return x

_drawn_inputs = setup_inputs


def setup_inputs(seed=0):
    import zlib

    import numpy as np

    out = dict(_drawn_inputs(seed))
    spreads = {'L0_gnn_bq': (0.0, 0.337),
     'L0_gnn_bk': (0.0, 0.8),
     'L0_gnn_bv': (0.0, 0.1),
     'L0_gnn_bf': (0.0, 0.1)}
    factors = {}
    for name, (base, spread) in spreads.items():
        noise = np.random.default_rng([zlib.crc32(name.encode()), seed]).standard_normal(out[name].shape)
        drawn = base * np.exp(spread * noise) if base else spread * noise
        out[name] = jnp.asarray(drawn.astype(out[name].dtype))
    for name, factor in factors.items():
        out[name] = (out[name] * factor).astype(out[name].dtype)
    return out
```

```python
from contextlib import ExitStack

import concourse.bass as bass
from concourse import mybir

F32 = mybir.dt.float32
F32R = mybir.dt.float32r
U8 = mybir.dt.uint8
ALU = mybir.AluOpType
ACT = mybir.ActivationFunctionType

GRAPHS, TOK, HID = 128, 128, 384
HEAD = 64
HEADS = HID // HEAD
CH = HID // 128
GROUP = 2
RING = 4
NEG = -9000000000000000.0
EPS = 1e-05
FLOAT_MAX = 3.4028234663852886e38
FIRST, LAST = -5, GRAPHS + 2
LOOP_FROM, LOOP_TO = RING, GRAPHS - 2 * RING
QK_FIRST = 14


class Slot:

    def __init__(self, n, j, near, turns):
        self.n, self.j, self.near, self.turns = n, j, near, turns

    def at(self, d):
        return self.n + d if self.near is None else self.near[self.j + d]

    def turn(self, d, ring):
        if self.turns is None:
            return 16 * ((self.n + d) // ring) + 16
        return self.turns[ring, (self.j + d) // ring]

    def has(self, d):
        return self.near is not None or 0 <= self.n + d < GRAPHS

    def after(self, d):
        return self.near is not None or self.n >= d

    def qk(self):
        return self.near is not None or -2 <= self.n < GRAPHS - 2

    def half(self, d):
        return (self.j + d) % 2

    def parity(self, d):
        return (self.j + d) % 4 // 2


def slots(engine, slot, near, turns=()):
    for n in range(FIRST, LOOP_FROM):
        slot(Slot(n, n % RING, None, None))
    with engine.Fori(LOOP_FROM, LOOP_TO, RING) as base:
        counts = {d: engine.snap(base + d) for d in near}
        dma = {(ring, k): engine.snap(base * (16 // ring) + (16 * k + 16)) for ring, k in turns}
        for j in range(RING):
            slot(Slot(base, j, counts, dma))
    for n in range(LOOP_TO, LAST):
        slot(Slot(n, n % RING, None, None))


def long_met(engine, s, semaphore, value):
    if s.near is not None:
        engine.wait_ge(semaphore, value)


def build(nc, x, adj, Wq, bq, Wk, bk, Wv, bv, Wf, bf, out):
    with ExitStack() as ctx:
        def sb(name, shape, dt=F32):
            return ctx.enter_context(nc.sbuf_tensor(name, shape, dt))

        def ps(name, shape):
            return ctx.enter_context(nc.psum_tensor(name, shape, F32))

        def sem(name):
            return ctx.enter_context(nc.semaphore(name))

        stage = {w: sb(f"stage_{w}", [128, CH, HID]) for w in "qkvf"}
        w_hi = {w: sb(f"w{w}_hi", [128, CH, HID], F32R) for w in "qkvf"}
        w_lo = {w: sb(f"w{w}_lo", [128, CH, HID], F32R) for w in "qkvf"}
        b_col = {w: sb(f"b{w}_col", [128, CH]) for w in "qkv"}
        bf_row = sb("bf_row", [128, HID])
        out_bias = sb("out_bias", [128, HID])
        bv_rows = sb("bv_rows", [128, CH, 128])
        ident = sb("ident", [128, 128])
        minus_half = sb("minus_half", [128, 1])

        x_in = sb("x_in", [TOK, RING, HID])
        x_bf = sb("x_bf", [TOK, RING, HID])
        adj_in = sb("adj_in", [TOK, RING, TOK], U8)
        edge_bias = sb("edge_bias", [TOK, 2, TOK])
        xt_hi = sb("xt_hi", [128, 2, CH, GROUP * TOK], F32R)
        xt_lo = sb("xt_lo", [128, 2, CH, GROUP * TOK], F32R)
        q_hi = sb("q_hi", [128, 2, CH, GROUP * TOK], F32R)
        q_lo = sb("q_lo", [128, 2, CH, GROUP * TOK], F32R)
        k_hi = sb("k_hi", [128, 2, CH, GROUP, 2 * TOK], F32R)
        k_lo = sb("k_lo", [128, 2, CH, GROUP, 2 * TOK], F32R)
        v_hi = sb("v_hi", [TOK, 2, HID], F32R)
        v_lo = sb("v_lo", [TOK, 2, HID], F32R)
        neg_scores = sb("neg_scores", [TOK, HEADS * TOK])
        neg_max = sb("neg_max", [TOK, 2, HEADS])
        probs = sb("probs", [TOK, 2, HEADS * TOK])
        prob_sum = sb("prob_sum", [TOK, 2, HEADS])
        prob_inv = sb("prob_inv", [TOK, 2, HEADS])
        pt_hi = sb("pt_hi", [TOK, HEADS * TOK], F32R)
        pt_lo = sb("pt_lo", [TOK, HEADS * TOK], F32R)
        ctx_hi = sb("ctx_hi", [128, CH, TOK], F32R)
        ctx_lo = sb("ctx_lo", [128, CH, TOK], F32R)
        resid = sb("resid", [TOK, 2, HID])
        stats = sb("stats", [TOK, 6])
        mean_var = sb("mean_var", [TOK, 2, 2])
        var_eps = sb("var_eps", [TOK, 2])
        rstd = sb("rstd", [TOK, 2])
        normed = sb("normed", [TOK, 2, HID])

        sc_ps = ps("sc_ps", [TOK, 1024])
        pc_ps = ps("pc_ps", [128, 1024])
        a_ps = ps("a_ps", [128, 512])
        b_ps = ps("b_ps", [128, 512])
        o_ps = ps("o_ps", [TOK, 512])
        x_ps = ps("x_ps", [128, 512])

        w_loaded = {w: sem(f"w{w}_loaded") for w in "qkvf"}
        biases_loaded = sem("biases_loaded")
        ident_zeroed, ident_made, consts_made = sem("ident_zeroed"), sem("ident_made"), sem("consts_made")
        keys_zeroed = sem("keys_zeroed")
        q_scaled = sem("q_scaled")
        ones_made, bv_repeated, bv_projected = sem("ones_made"), sem("bv_repeated"), sem("bv_projected")
        out_bias_made = sem("out_bias_made")
        w_hi_made, w_lo_made = sem("w_hi_made"), sem("w_lo_made")
        x_loaded = [sem(f"x_loaded{j}") for j in range(RING)]
        adj_loaded = [sem(f"adj_loaded{j}") for j in range(RING)]
        stored = [sem(f"stored{j}") for j in range(2)]
        scores_done = [sem(f"scores_done{i}") for i in range(2)]
        pt_done = [sem(f"pt_done{i}") for i in range(2)]
        qk_done = [sem(f"qk_done{c}") for c in range(CH)]
        ctx_done, proj_done, xt_done, v_done = sem("ctx_done"), sem("proj_done"), sem("xt_done"), sem("v_done")
        exp_done = sem("exp_done")
        pt_hi_done = [sem(f"pt_hi_done{i}") for i in range(2)]
        qk_hi_done = [sem(f"qk_hi_done{c}") for c in range(CH)]
        ctx_hi_done, xt_hi_done, v_hi_done = sem("ctx_hi_done"), sem("xt_hi_done"), sem("v_hi_done")
        masked = [sem(f"masked{p}") for p in range(CH)]
        pt_lo_done = [sem(f"pt_lo_done{i}") for i in range(2)]
        qk_lo_done = [sem(f"qk_lo_done{c}") for c in range(CH)]
        ctx_lo_done, xt_lo_done, v_lo_done = sem("ctx_lo_done"), sem("xt_lo_done"), sem("v_lo_done")
        inv_done, resid_done, stats_done = sem("inv_done"), sem("resid_done"), sem("stats_done")
        mean_done, normed_done = sem("mean_done"), sem("normed_done")
        edges_done, x_bf_done, probs_done = sem("edges_done"), sem("x_bf_done"), sem("probs_done")
        eps_added, rstd_done = sem("eps_added"), sem("rstd_done")

        block = ctx.enter_context(nc.Block())


        @block.sync
        def _(sp):
            for w, W in (("q", Wq), ("k", Wk), ("v", Wv), ("f", Wf)):
                sp.dma_start(stage[w][:], W.rearrange("(c p) n -> p c n", p=128)).then_inc(w_loaded[w], 16)
            for w, b in (("q", bq), ("k", bk), ("v", bv)):
                sp.dma_start(b_col[w][:], b.rearrange("(c p) -> p c", p=128),
                             allow_slow_non_contiguous=True).then_inc(biases_loaded, 16)
            sp.dma_start(bf_row[:], bf.rearrange("(a n) -> a n", a=1).partition_broadcast(128)).then_inc(biases_loaded, 16)

            def slot(s):
                if s.has(5):
                    jx = (s.j + 1) % RING
                    if s.after(-1):
                        long_met(sp, s, x_loaded[jx], 16)
                        sp.wait_ge(xt_done, s.at(2))
                        sp.wait_ge(x_bf_done, s.at(2))
                    sp.dma_start(x_in[:, jx, :], x[s.at(5)]).then_inc(x_loaded[jx], 16)
                if s.has(4):
                    if s.after(0):
                        long_met(sp, s, adj_loaded[s.j], 16)
                        sp.wait_ge(edges_done, s.at(1))
                    sp.dma_start(adj_in[:, s.j, :], adj[s.at(4)]).then_inc(adj_loaded[s.j], 16)
                if s.has(-2):
                    long_met(sp, s, stored[s.half(0)], 16)
                    sp.wait_ge(normed_done, s.at(-1))
                    sp.dma_start(out[s.at(-2)], normed[:, s.half(0), :]).then_inc(stored[s.half(0)], 16)

            slots(sp, slot, near=range(-2, 9))
            for j in range(2):
                sp.wait_ge(stored[j], 16 * GRAPHS // 2)

        @block.gpsimd
        def _(pool):
            nc.gpsimd.memset(ident[:], 0.0).then_inc(ident_zeroed, 1)
            pool.wait_ge(ident_zeroed, 1)
            nc.gpsimd.affine_select(out=ident[:], in_=ident[:], compare_op=ALU.not_equal, fill=1.0, base=0,
                                    pattern=[[-1, 128]], channel_multiplier=1).then_inc(ident_made, 1)
            nc.gpsimd.memset(minus_half[:], -0.5).then_inc(consts_made, 1)
            pool.wait_ge(consts_made, 1)
            pool.wait_ge(out_bias_made, 1)

            def slot(s):
                if s.has(2):
                    jb = (s.j + 2) % RING
                    pool.wait_ge(x_loaded[jb], s.turn(2, RING))
                    if s.after(2):
                        pool.wait_ge(resid_done, s.at(-1))
                    nc.gpsimd.tensor_tensor(x_bf[:, jb, :], x_in[:, jb, :], out_bias[:], ALU.add).then_inc(x_bf_done, 1)
                if s.has(1):
                    ja = (s.j + 1) % RING
                    long_met(pool, s, adj_loaded[ja], 16)
                    pool.wait_ge(adj_loaded[ja], s.turn(1, RING))
                    if s.after(1):
                        pool.wait_ge(masked[CH - 1], s.at(0))
                    nc.gpsimd.tensor_scalar(edge_bias[:, s.half(1), :], adj_in[:, ja, :], -1.0, -NEG,
                                            ALU.add, ALU.mult).then_inc(edges_done, 1)
                if s.has(0):
                    pool.wait_ge(inv_done, s.at(1))
                    p = probs[:, s.half(0), :].rearrange("q (h k) -> q h k", h=HEADS)
                    r = prob_inv[:, s.half(0), :].unsqueeze(2).to_broadcast([TOK, HEADS, TOK])
                    nc.gpsimd.tensor_tensor(p, p, r, ALU.mult).then_inc(probs_done, 1)
                if s.has(-1):
                    h = s.half(1)
                    long_met(pool, s, mean_done, 1)
                    pool.wait_ge(mean_done, s.at(0))
                    nc.gpsimd.tensor_scalar(var_eps[:, h:h + 1], mean_var[:, h, 1:2], EPS, None,
                                            ALU.add).then_inc(eps_added, 1)
                    pool.wait_ge(eps_added, s.at(0))
                    nc.gpsimd.tensor_tensor(rstd[:, h:h + 1], var_eps[:, h:h + 1], minus_half[:],
                                            ALU.pow).then_inc(rstd_done, 1)

            slots(pool, slot, near=range(-1, 6), turns=((RING, 0), (RING, 1)))

        @block.scalar
        def _(act):
            pc3 = pc_ps[:, 0:CH * 256].rearrange("p (c n) -> p c n", c=CH)
            for i, w in enumerate("qkvf"):
                if w == "q":
                    act.wait_ge(q_scaled, 1)
                else:
                    act.wait_ge(w_loaded[w], 16)
                nc.scalar.copy(w_hi[w][:], stage[w][:]).then_inc(w_hi_made, 1)
            act.wait_ge(q_scaled, 2)
            act.wait_ge(biases_loaded, 64)

            def exps(s, p):
                act.wait_ge(masked[p], s.at(1))
                for h in (2 * p, 2 * p + 1):
                    cols = slice(h * TOK, (h + 1) * TOK)
                    last = nc.scalar.activation(probs[:, s.half(0), cols], neg_scores[:, cols], ACT.Exp, scale=-1.0,
                                         bias=neg_max[:, s.half(0), h:h + 1],
                                         accum_out=prob_sum[:, s.half(0), h:h + 1])
                if p == CH - 1:
                    last.then_inc(exp_done, 1)

            def qk_hi(s, c):
                par = s.parity(2)
                src = (b_ps if c == 1 else a_ps)[:, 0:GROUP * TOK]
                act.wait_ge(qk_done[c], s.at(3))
                if s.j % 2 == 0:
                    nc.scalar.activation(q_hi[:, par, c, :], src, ACT.Identity,
                                         bias=b_col["q"][:, c:c + 1]).then_inc(qk_hi_done[c], 1)
                else:
                    for h in range(2):
                        rows = slice(HEAD * h, HEAD * (h + 1))
                        last = nc.scalar.activation(
                            k_hi[rows, par, c, :, h * TOK:(h + 1) * TOK],
                            src[rows, :].rearrange("p (g t) -> p g t", g=GROUP), ACT.Identity,
                            bias=b_col["k"][rows, c:c + 1])
                    last.then_inc(qk_hi_done[c], 1)

            def slot(s):
                if s.has(-1):
                    for part, cols in enumerate((slice(0, 512), slice(512, 768))):
                        act.wait_ge(pt_done[part], s.at(0))
                        nc.scalar.copy(pt_hi[:, cols], pc_ps[:, cols]).then_inc(pt_hi_done[part], 1)
                if s.has(0):
                    exps(s, 0)
                if s.qk():
                    qk_hi(s, 0)
                if s.has(0):
                    exps(s, 1)
                if s.qk():
                    qk_hi(s, 1)
                if s.has(-1):
                    act.wait_ge(ctx_done, s.at(0))
                    for h in range(2):
                        rows = slice(HEAD * h, HEAD * (h + 1))
                        last = nc.scalar.copy(ctx_hi[rows], pc3[rows, :, h * TOK:(h + 1) * TOK])
                    last.then_inc(ctx_hi_done, 1)
                if s.has(0):
                    exps(s, 2)
                if s.qk():
                    qk_hi(s, 2)
                if s.has(4):
                    act.wait_ge(xt_done, s.at(5))
                    nc.scalar.copy(xt_hi[:, s.parity(0), :, s.half(0) * TOK:(s.half(0) + 1) * TOK],
                                   x_ps[:, 0:HID].rearrange("p (c t) -> p c t", c=CH)).then_inc(xt_hi_done, 1)
                if s.has(1):
                    act.wait_ge(v_done, s.at(2))
                    nc.scalar.copy(v_hi[:, s.half(1), :], b_ps[:, 0:HID]).then_inc(v_hi_done, 1)

            slots(act, slot, near=range(0, 9))

        @block.vector
        def _(dve):
            pc3 = pc_ps[:, 0:CH * 256].rearrange("p (c n) -> p c n", c=CH)
            k_zero = [t[rows, :, :, :, cols] for t in (k_hi, k_lo)
                      for rows, cols in ((slice(0, 64), slice(TOK, 2 * TOK)), (slice(64, 128), slice(0, TOK)))]
            for t in k_zero:
                for par in range(2):
                    last = nc.vector.memset(t[:, par].rearrange("p c g k -> p (c g) k").bitcast(F32), 0.0)
            last.then_inc(keys_zeroed, 1)
            dve.wait_ge(w_loaded["q"], 16)
            nc.vector.tensor_scalar(stage["q"][:], stage["q"][:], 0.125, None, ALU.mult).then_inc(q_scaled, 1)
            dve.wait_ge(biases_loaded, 64)
            nc.vector.tensor_scalar(b_col["q"][:], b_col["q"][:], 0.125, None, ALU.mult).then_inc(q_scaled, 1)
            nc.vector.memset(bv_rows[:], 1.0).then_inc(ones_made, 1)
            dve.wait_ge(ones_made, 1)
            for c in range(CH):
                nc.vector.tensor_scalar(bv_rows[:, c, :], bv_rows[:, c, :], b_col["v"][:, c:c + 1], None,
                                        ALU.mult).then_inc(bv_repeated, 1)
            for i, w in enumerate("qkvf"):
                dve.wait_ge(w_hi_made, i + 1)
                nc.vector.tensor_tensor(w_lo[w][:], stage[w][:], w_hi[w][:].bitcast(F32),
                                        ALU.subtract).then_inc(w_lo_made, 1)
            dve.wait_ge(bv_projected, 1)
            nc.vector.tensor_tensor(out_bias[:], o_ps[:, 0:HID], bf_row[:], ALU.add).then_inc(out_bias_made, 1)

            def masked_max(s, p):
                for h in (2 * p, 2 * p + 1):
                    cols = slice(h * TOK, (h + 1) * TOK)
                    last = nc.vector.tensor_tensor_reduce(
                        out=neg_scores[:, cols], in0=sc_ps[:, cols], in1=edge_bias[:, s.half(0), :], scale=-1.0,
                        scalar=FLOAT_MAX, op0=ALU.add, op1=ALU.min,
                        accum_out=neg_max[:, s.half(0), h:h + 1])
                last.then_inc(masked[p], 1)

            def qk_lo(s, c):
                par = s.parity(2)
                src = (b_ps if c == 1 else a_ps)[:, 0:GROUP * TOK]
                dve.wait_ge(qk_hi_done[c], s.at(3))
                if s.j % 2 == 0:
                    nc.vector.scalar_tensor_tensor(out=q_lo[:, par, c, :], in0=src, scalar=b_col["q"][:, c:c + 1],
                                                   in1=q_hi[:, par, c, :].bitcast(F32), op0=ALU.add,
                                                   op1=ALU.subtract).then_inc(qk_lo_done[c], 1)
                else:
                    for h in range(2):
                        rows, cols = slice(HEAD * h, HEAD * (h + 1)), slice(h * TOK, (h + 1) * TOK)
                        last = nc.vector.scalar_tensor_tensor(
                            out=k_lo[rows, par, c, :, cols], in0=src[rows, :].rearrange("p (g t) -> p g t", g=GROUP),
                            scalar=b_col["k"][rows, c:c + 1], in1=k_hi[rows, par, c, :, cols].bitcast(F32),
                            op0=ALU.add, op1=ALU.subtract)
                    last.then_inc(qk_lo_done[c], 1)

            def slot(s):
                if s.has(0):
                    dve.wait_ge(edges_done, s.at(1))
                if s.has(-2):
                    h = s.half(0)
                    dve.wait_ge(rstd_done, s.at(-1))
                    if s.after(4):
                        dve.wait_ge(stored[h], s.turn(-4, 2))
                    nc.vector.tensor_scalar(normed[:, h, :], resid[:, h, :], mean_var[:, h, 0:1], rstd[:, h:h + 1],
                                            ALU.subtract, ALU.mult).then_inc(normed_done, 1)
                if s.has(0):
                    long_met(dve, s, keys_zeroed, 1)
                    if s.after(1):
                        dve.wait_ge(exp_done, s.at(0))
                    dve.wait_ge(scores_done[0], s.at(1))
                    masked_max(s, 0)
                    masked_max(s, 1)
                    long_met(dve, s, keys_zeroed, 1)
                    dve.wait_ge(scores_done[1], s.at(1))
                    masked_max(s, 2)
                if s.has(-1):
                    for part, cols in enumerate((slice(0, 512), slice(512, 768))):
                        dve.wait_ge(pt_hi_done[part], s.at(0))
                        nc.vector.tensor_tensor(pt_lo[:, cols], pc_ps[:, cols], pt_hi[:, cols].bitcast(F32),
                                                ALU.subtract).then_inc(pt_lo_done[part], 1)
                if s.qk():
                    qk_lo(s, 0)
                    qk_lo(s, 1)
                if s.has(-1):
                    dve.wait_ge(ctx_hi_done, s.at(0))
                    for h in range(2):
                        rows = slice(HEAD * h, HEAD * (h + 1))
                        last = nc.vector.tensor_tensor(ctx_lo[rows], pc3[rows, :, h * TOK:(h + 1) * TOK],
                                                       ctx_hi[rows].bitcast(F32), ALU.subtract)
                    last.then_inc(ctx_lo_done, 1)
                if s.has(0):
                    dve.wait_ge(exp_done, s.at(1))
                    nc.vector.reciprocal(prob_inv[:, s.half(0), :], prob_sum[:, s.half(0), :]).then_inc(inv_done, 1)
                if s.qk():
                    qk_lo(s, 2)
                if s.has(-1):
                    h = s.half(1)
                    dve.wait_ge(proj_done, s.at(0))
                    dve.wait_ge(x_bf_done, s.at(0))
                    nc.vector.tensor_tensor(resid[:, h, :], o_ps[:, 0:HID], x_bf[:, (s.j - 1) % RING, :],
                                            ALU.add).then_inc(resid_done, 1)
                if s.has(4):
                    dve.wait_ge(xt_hi_done, s.at(5))
                    cols = slice(s.half(0) * TOK, (s.half(0) + 1) * TOK)
                    nc.vector.tensor_tensor(xt_lo[:, s.parity(0), :, cols],
                                            x_ps[:, 0:HID].rearrange("p (c t) -> p c t", c=CH),
                                            xt_hi[:, s.parity(0), :, cols].bitcast(F32),
                                            ALU.subtract).then_inc(xt_lo_done, 1)
                if s.has(-1):
                    dve.wait_ge(resid_done, s.at(0))
                    nc.vector.bn_stats(stats[:], resid[:, s.half(1), :]).then_inc(stats_done, 1)
                if s.has(1):
                    dve.wait_ge(v_hi_done, s.at(2))
                    nc.vector.tensor_tensor(v_lo[:, s.half(1), :], b_ps[:, 0:HID],
                                            v_hi[:, s.half(1), :].bitcast(F32), ALU.subtract).then_inc(v_lo_done, 1)
                if s.has(-1):
                    long_met(dve, s, stats_done, 1)
                    dve.wait_ge(stats_done, s.at(0))
                    nc.vector.bn_aggr(mean_var[:, s.half(1), :], stats[:]).then_inc(mean_done, 1)

            slots(dve, slot, near=range(-1, 9), turns=((2, -2), (2, -1)))

        @block.tensor
        def _(pe):
            def product(out_ps, pairs):
                for i, (s_hi, s_lo, m_hi, m_lo) in enumerate(pairs):
                    nc.tensor.matmul(out_ps, s_hi, m_hi, start=(i == 0), stop=False)
                    nc.tensor.matmul(out_ps, s_lo, m_hi, start=False, stop=False)
                    last = nc.tensor.matmul(out_ps, s_hi, m_lo, start=False, stop=(i == len(pairs) - 1))
                return last

            def scores(s):
                par = s.parity(0)
                here = slice(s.half(0) * TOK, (s.half(0) + 1) * TOK)
                pe.wait_ge(qk_lo_done[CH - 1], s.at(2 if s.j % 2 == 0 else 1))
                if s.after(1):
                    pe.wait_ge(masked[CH - 1], s.at(0))
                for p in range(CH):
                    last = product(sc_ps[:, p * 256:(p + 1) * 256],
                                   [(q_hi[:, par, p, here], q_lo[:, par, p, here],
                                     k_hi[:, par, p, s.half(0), :], k_lo[:, par, p, s.half(0), :])])
                    if p >= 1:
                        last.then_inc(scores_done[p - 1], 1)

            def transposed_probs(s):
                pe.wait_ge(probs_done, s.at(0))
                if s.after(2):
                    pe.wait_ge(ctx_lo_done, s.at(-1))
                for h in range(HEADS):
                    cols = slice(h * TOK, (h + 1) * TOK)
                    last = nc.tensor.transpose(pc_ps[:, cols], probs[:, s.half(1), cols], ident[:])
                    if h in (3, HEADS - 1):
                        last.then_inc(pt_done[h // 4], 1)

            def qk_products(s, first, last):
                w, par = "qk"[s.j % 2], s.parity(2)
                for i in range(first, last):
                    c, k = i // 9, i % 9
                    ci, term = k // 3, k % 3
                    if k == 0:
                        if c == 0:
                            if s.after(-1):
                                pe.wait_ge(qk_lo_done[2], s.at(2))
                            if s.j % 2 == 0:
                                pe.wait_ge(xt_lo_done, s.at(4))
                        elif c == 1:
                            if s.after(0):
                                pe.wait_ge(v_lo_done, s.at(1))
                            elif s.after(-1):
                                pe.wait_ge(qk_lo_done[1], s.at(2))
                        else:
                            pe.wait_ge(qk_lo_done[0], s.at(3))
                    stationary = (w_lo if term == 1 else w_hi)[w][:, ci, c * 128:(c + 1) * 128]
                    moving = (xt_lo if term == 2 else xt_hi)[:, par, ci, :]
                    mm = nc.tensor.matmul((b_ps if c == 1 else a_ps)[:, 0:GROUP * TOK], stationary, moving, start=(k == 0),
                                          stop=(k == 8), skip_group_check=True)
                    if k == 8:
                        mm.then_inc(qk_done[c], 1)

            def context(s):
                v = s.half(1)
                pe.wait_ge(pt_lo_done[0], s.at(0))
                pe.wait_ge(pt_lo_done[1], s.at(0))
                pe.wait_ge(v_lo_done, s.at(0))
                for p in range(CH):
                    two = slice(p * 128, (p + 1) * 128)
                    moving = slice(p * 256, (p + 1) * 256)
                    last = product(pc_ps[:, moving],
                                   [(v_hi[:, v, two], v_lo[:, v, two], pt_hi[:, moving], pt_lo[:, moving])])
                last.then_inc(ctx_done, 1)

            def projection(s):
                pe.wait_ge(ctx_lo_done, s.at(0))
                if s.after(2):
                    pe.wait_ge(resid_done, s.at(-1))
                product(o_ps[:, 0:HID], [(ctx_hi[:, c, :], ctx_lo[:, c, :], w_hi["f"][:, c, :], w_lo["f"][:, c, :])
                                         for c in range(CH)]).then_inc(proj_done, 1)

            def transposed_x(s):
                pe.wait_ge(x_loaded[s.j], s.turn(4, RING))
                if s.after(-3):
                    pe.wait_ge(xt_lo_done, s.at(4))
                for c in range(CH):
                    cols = slice(c * 128, (c + 1) * 128)
                    last = nc.tensor.transpose(x_ps[:, cols], x_in[:, s.j, cols], ident[:])
                last.then_inc(xt_done, 1)

            def values(s):
                here = slice(s.half(1) * TOK, (s.half(1) + 1) * TOK)
                par = s.parity(1)
                if s.qk():
                    pe.wait_ge(qk_lo_done[1], s.at(3))
                else:
                    pe.wait_ge(v_lo_done, s.at(1))
                product(b_ps[:, 0:HID], [(xt_hi[:, par, c, here], xt_lo[:, par, c, here], w_hi["v"][:, c, :],
                                          w_lo["v"][:, c, :]) for c in range(CH)]).then_inc(v_done, 1)

            pe.wait_ge(ident_made, 1)
            pe.wait_ge(keys_zeroed, 1)
            pe.wait_ge(bv_repeated, CH)
            pe.wait_ge(w_loaded["f"], 16)
            for c in range(CH):
                last = nc.tensor.matmul(o_ps[:, 0:HID], bv_rows[:, c, :], stage["f"][:, c, :], start=(c == 0),
                                        stop=(c == CH - 1))
            last.then_inc(bv_projected, 1)
            pe.wait_ge(out_bias_made, 1)
            pe.wait_ge(w_lo_made, 4)

            def slot(s):
                if s.has(0):
                    scores(s)
                if s.has(-1):
                    transposed_probs(s)
                if s.qk():
                    qk_products(s, 0, QK_FIRST)
                if s.has(-1):
                    context(s)
                if s.qk():
                    qk_products(s, QK_FIRST, 27)
                if s.has(-1):
                    projection(s)
                if s.has(4):
                    transposed_x(s)
                if s.has(1):
                    values(s)

            slots(pe, slot, near=range(-1, 8), turns=((RING, 1),))


_INS = ["x", "adj"] + [f"L0_gnn_{n}" for n in ("Wq", "bq", "Wk", "bk", "Wv", "bv", "Wf", "bf")]


def kernel(**inputs):
    import numpy as _np
    import concourse.bacc as _bacc
    from concourse import mybir as _mybir
    from concourse.bass_utils import run_bass_kernel_spmd as _run

    nc = _bacc.Bacc("TRN2", target_bir_lowering=False, num_devices=1)
    arrays, args = {}, []
    for name in _INS:
        a = _np.ascontiguousarray(inputs[name])
        arrays[f"in_{name}_dram"] = a
        args.append(nc.dram_tensor(f"in_{name}_dram", a.shape, _mybir.dt.from_np(a.dtype), kind="ExternalInput").ap())
    args.append(nc.dram_tensor("out_dram", (GRAPHS, TOK, HID), F32, kind="ExternalOutput").ap())
    build(nc, *args)
    r = _run(nc, [arrays], core_ids=[0])
    return r.results[0]["out_dram"]
```

```python
from contextlib import ExitStack

import concourse.bass as bass
from concourse import mybir

F32 = mybir.dt.float32
F32R = mybir.dt.float32r
U8 = mybir.dt.uint8
ALU = mybir.AluOpType
ACT = mybir.ActivationFunctionType

GRAPHS, TOK, HID = 128, 128, 384
HEAD = 64
HEADS = HID // HEAD
CH = HID // 128
GROUP = 2
RING = 4
NEG = -9000000000000000.0
EPS = 1e-05
FLOAT_MAX = 3.4028234663852886e38
FIRST, LAST = -5, GRAPHS + 2
LOOP_FROM, LOOP_TO = RING, GRAPHS - 2 * RING
QK_CHUNKS = ((("q", 0), ("k", 0), ("q", 1)), (("k", 1), ("q", 2), ("k", 2)))


class Slot:

    def __init__(self, n, j, near, turns):
        self.n, self.j, self.near, self.turns = n, j, near, turns

    def at(self, d):
        return self.n + d if self.near is None else self.near[self.j + d]

    def turn(self, d, ring):
        if self.turns is None:
            return 16 * ((self.n + d) // ring) + 16
        return self.turns[ring, (self.j + d) // ring]

    def has(self, d):
        return self.near is not None or 0 <= self.n + d < GRAPHS

    def after(self, d):
        return self.near is not None or self.n >= d

    def qk(self):
        return self.near is not None or -2 <= self.n < GRAPHS - 2

    def half(self, d):
        return (self.j + d) % 2

    def parity(self, d):
        return (self.j + d) % 4 // 2


def slots(engine, slot, near, turns=()):
    for n in range(FIRST, LOOP_FROM):
        slot(Slot(n, n % RING, None, None))
    with engine.Fori(LOOP_FROM, LOOP_TO, RING) as base:
        counts = {d: engine.snap(base + d) for d in near}
        dma = {(ring, k): engine.snap(base * (16 // ring) + (16 * k + 16)) for ring, k in turns}
        for j in range(RING):
            slot(Slot(base, j, counts, dma))
    for n in range(LOOP_TO, LAST):
        slot(Slot(n, n % RING, None, None))


def long_met(engine, s, semaphore, value):
    if s.near is not None:
        engine.wait_ge(semaphore, value)


def build(nc, x, adj, Wq, bq, Wk, bk, Wv, bv, Wf, bf, out):
    with ExitStack() as ctx:
        def sb(name, shape, dt=F32):
            return ctx.enter_context(nc.sbuf_tensor(name, shape, dt))

        def ps(name, shape):
            return ctx.enter_context(nc.psum_tensor(name, shape, F32))

        def sem(name):
            return ctx.enter_context(nc.semaphore(name))

        stage = {w: sb(f"stage_{w}", [128, CH, HID]) for w in "qkvf"}
        w_hi = {w: sb(f"w{w}_hi", [128, CH, HID], F32R) for w in "qkvf"}
        w_lo = {w: sb(f"w{w}_lo", [128, CH, HID], F32R) for w in "qkvf"}
        b_col = {w: sb(f"b{w}_col", [128, CH]) for w in "qkv"}
        bf_row = sb("bf_row", [128, HID])
        out_bias = sb("out_bias", [128, HID])
        bv_rows = sb("bv_rows", [128, CH, 128])
        ident = sb("ident", [128, 128])
        minus_half = sb("minus_half", [128, 1])

        x_in = sb("x_in", [TOK, RING, HID])
        x_bf = sb("x_bf", [TOK, RING, HID])
        adj_in = sb("adj_in", [TOK, RING, TOK], U8)
        edge_bias = sb("edge_bias", [TOK, 2, TOK])
        xt_hi = sb("xt_hi", [128, 2, CH, GROUP * TOK], F32R)
        xt_lo = sb("xt_lo", [128, 2, CH, GROUP * TOK], F32R)
        q_hi = sb("q_hi", [128, 2, CH, GROUP * TOK], F32R)
        q_lo = sb("q_lo", [128, 2, CH, GROUP * TOK], F32R)
        k_hi = sb("k_hi", [128, 2, CH, GROUP, 2 * TOK], F32R)
        k_lo = sb("k_lo", [128, 2, CH, GROUP, 2 * TOK], F32R)
        v_hi = sb("v_hi", [TOK, 2, HID], F32R)
        v_lo = sb("v_lo", [TOK, 2, HID], F32R)
        neg_scores = sb("neg_scores", [TOK, HEADS * TOK])
        neg_max = sb("neg_max", [TOK, 2, HEADS])
        probs = sb("probs", [TOK, 2, HEADS * TOK])
        prob_sum = sb("prob_sum", [TOK, 2, HEADS])
        prob_inv = sb("prob_inv", [TOK, 2, HEADS])
        pt_hi = sb("pt_hi", [TOK, HEADS * TOK], F32R)
        pt_lo = sb("pt_lo", [TOK, HEADS * TOK], F32R)
        ctx_hi = sb("ctx_hi", [128, CH, TOK], F32R)
        ctx_lo = sb("ctx_lo", [128, CH, TOK], F32R)
        resid = sb("resid", [TOK, 2, HID])
        stats = sb("stats", [TOK, 6])
        mean_var = sb("mean_var", [TOK, 2, 2])
        var_eps = sb("var_eps", [TOK, 2])
        rstd = sb("rstd", [TOK, 2])
        normed = sb("normed", [TOK, 2, HID])

        sc_ps = ps("sc_ps", [TOK, 1024])
        pc_ps = ps("pc_ps", [128, 1024])
        a_ps = ps("a_ps", [128, 512])
        b_ps = ps("b_ps", [128, 512])
        c_ps = ps("c_ps", [128, 512])
        o_ps = ps("o_ps", [TOK, 512])
        qk_ps = (a_ps, b_ps, c_ps)

        w_loaded = {w: sem(f"w{w}_loaded") for w in "qkvf"}
        biases_loaded = sem("biases_loaded")
        ident_zeroed, ident_made, consts_made = sem("ident_zeroed"), sem("ident_made"), sem("consts_made")
        keys_zeroed = sem("keys_zeroed")
        q_scaled = sem("q_scaled")
        ones_made, bv_repeated, bv_projected = sem("ones_made"), sem("bv_repeated"), sem("bv_projected")
        out_bias_made = sem("out_bias_made")
        w_hi_made, w_lo_made = sem("w_hi_made"), sem("w_lo_made")
        x_loaded = [sem(f"x_loaded{j}") for j in range(RING)]
        adj_loaded = [sem(f"adj_loaded{j}") for j in range(RING)]
        stored = [sem(f"stored{j}") for j in range(2)]
        scores_done = [sem(f"scores_done{i}") for i in range(2)]
        pt_done = [sem(f"pt_done{i}") for i in range(2)]
        qk_done = [sem(f"qk_done{c}") for c in range(CH)]
        ctx_done, proj_done, xt_done, v_done = sem("ctx_done"), sem("proj_done"), sem("xt_done"), sem("v_done")
        exp_done = sem("exp_done")
        pt_hi_done = [sem(f"pt_hi_done{i}") for i in range(2)]
        qk_hi_done = [sem(f"qk_hi_done{c}") for c in range(CH)]
        ctx_hi_done, xt_hi_done, v_hi_done = sem("ctx_hi_done"), sem("xt_hi_done"), sem("v_hi_done")
        masked = [sem(f"masked{p}") for p in range(CH)]
        pt_lo_done = [sem(f"pt_lo_done{i}") for i in range(2)]
        qk_lo_done = [sem(f"qk_lo_done{c}") for c in range(CH)]
        ctx_lo_done, xt_lo_done, v_lo_done = sem("ctx_lo_done"), sem("xt_lo_done"), sem("v_lo_done")
        inv_done, resid_done, stats_done = sem("inv_done"), sem("resid_done"), sem("stats_done")
        mean_done, normed_done = sem("mean_done"), sem("normed_done")
        edges_done, x_bf_done, probs_done = sem("edges_done"), sem("x_bf_done"), sem("probs_done")
        eps_added, rstd_done = sem("eps_added"), sem("rstd_done")

        block = ctx.enter_context(nc.Block())


        @block.sync
        def _(sp):
            for w, W in (("q", Wq), ("k", Wk), ("v", Wv), ("f", Wf)):
                sp.dma_start(stage[w][:], W.rearrange("(c p) n -> p c n", p=128)).then_inc(w_loaded[w], 16)
            for w, b in (("q", bq), ("k", bk), ("v", bv)):
                sp.dma_start(b_col[w][:], b.rearrange("(c p) -> p c", p=128),
                             allow_slow_non_contiguous=True).then_inc(biases_loaded, 16)
            sp.dma_start(bf_row[:], bf.rearrange("(a n) -> a n", a=1).partition_broadcast(128)).then_inc(biases_loaded, 16)

            def slot(s):
                if s.has(5):
                    jx = (s.j + 1) % RING
                    if s.after(-1):
                        long_met(sp, s, x_loaded[jx], 16)
                        sp.wait_ge(xt_done, s.at(2))
                        sp.wait_ge(x_bf_done, s.at(2))
                    sp.dma_start(x_in[:, jx, :], x[s.at(5)]).then_inc(x_loaded[jx], 16)
                if s.has(4):
                    if s.after(0):
                        long_met(sp, s, adj_loaded[s.j], 16)
                        sp.wait_ge(edges_done, s.at(1))
                    sp.dma_start(adj_in[:, s.j, :], adj[s.at(4)]).then_inc(adj_loaded[s.j], 16)
                if s.has(-2):
                    long_met(sp, s, stored[s.half(0)], 16)
                    sp.wait_ge(normed_done, s.at(-1))
                    sp.dma_start(out[s.at(-2)], normed[:, s.half(0), :]).then_inc(stored[s.half(0)], 16)

            slots(sp, slot, near=range(-2, 9))
            for j in range(2):
                sp.wait_ge(stored[j], 16 * GRAPHS // 2)

        @block.gpsimd
        def _(pool):
            nc.gpsimd.memset(ident[:], 0.0).then_inc(ident_zeroed, 1)
            pool.wait_ge(ident_zeroed, 1)
            nc.gpsimd.affine_select(out=ident[:], in_=ident[:], compare_op=ALU.not_equal, fill=1.0, base=0,
                                    pattern=[[-1, 128]], channel_multiplier=1).then_inc(ident_made, 1)
            nc.gpsimd.memset(minus_half[:], -0.5).then_inc(consts_made, 1)
            pool.wait_ge(consts_made, 1)
            pool.wait_ge(out_bias_made, 1)

            def slot(s):
                if s.has(2):
                    jb = (s.j + 2) % RING
                    pool.wait_ge(x_loaded[jb], s.turn(2, RING))
                    if s.after(2):
                        pool.wait_ge(resid_done, s.at(-1))
                    nc.gpsimd.tensor_tensor(x_bf[:, jb, :], x_in[:, jb, :], out_bias[:], ALU.add).then_inc(x_bf_done, 1)
                if s.has(1):
                    ja = (s.j + 1) % RING
                    long_met(pool, s, adj_loaded[ja], 16)
                    pool.wait_ge(adj_loaded[ja], s.turn(1, RING))
                    if s.after(1):
                        pool.wait_ge(masked[CH - 1], s.at(0))
                    nc.gpsimd.tensor_scalar(edge_bias[:, s.half(1), :], adj_in[:, ja, :], -1.0, -NEG,
                                            ALU.add, ALU.mult).then_inc(edges_done, 1)
                if s.has(-2):
                    h = s.half(0)
                    long_met(pool, s, mean_done, 1)
                    pool.wait_ge(mean_done, s.at(-1))
                    nc.gpsimd.tensor_scalar(var_eps[:, h:h + 1], mean_var[:, h, 1:2], EPS, None,
                                            ALU.add).then_inc(eps_added, 1)
                    pool.wait_ge(eps_added, s.at(-1))
                    nc.gpsimd.tensor_tensor(rstd[:, h:h + 1], var_eps[:, h:h + 1], minus_half[:],
                                            ALU.pow).then_inc(rstd_done, 1)
                if s.has(0):
                    pool.wait_ge(inv_done, s.at(1))
                    p = probs[:, s.half(0), :].rearrange("q (h k) -> q h k", h=HEADS)
                    r = prob_inv[:, s.half(0), :].unsqueeze(2).to_broadcast([TOK, HEADS, TOK])
                    nc.gpsimd.tensor_tensor(p, p, r, ALU.mult).then_inc(probs_done, 1)

            slots(pool, slot, near=range(-1, 6), turns=((RING, 0), (RING, 1)))

        @block.scalar
        def _(act):
            pc3 = pc_ps[:, 0:CH * 256].rearrange("p (c n) -> p c n", c=CH)
            for i, w in enumerate("qkvf"):
                if w == "q":
                    act.wait_ge(q_scaled, 1)
                else:
                    act.wait_ge(w_loaded[w], 16)
                nc.scalar.copy(w_hi[w][:], stage[w][:]).then_inc(w_hi_made, 1)
            act.wait_ge(q_scaled, 2)
            act.wait_ge(biases_loaded, 64)

            def exps(s, p):
                act.wait_ge(masked[p], s.at(1))
                for h in (2 * p, 2 * p + 1):
                    cols = slice(h * TOK, (h + 1) * TOK)
                    last = nc.scalar.activation(probs[:, s.half(0), cols], neg_scores[:, cols], ACT.Exp, scale=-1.0,
                                         bias=neg_max[:, s.half(0), h:h + 1],
                                         accum_out=prob_sum[:, s.half(0), h:h + 1])
                if p == CH - 1:
                    last.then_inc(exp_done, 1)

            def qk_hi(s, i):
                par, (w, c) = s.parity(2), QK_CHUNKS[s.j % 2][i]
                src = qk_ps[i][:, 0:GROUP * TOK]
                act.wait_ge(qk_done[i], s.at(3))
                if w == "q":
                    nc.scalar.activation(q_hi[:, par, c, :], src, ACT.Identity,
                                         bias=b_col["q"][:, c:c + 1]).then_inc(qk_hi_done[i], 1)
                else:
                    for h in range(2):
                        rows = slice(HEAD * h, HEAD * (h + 1))
                        last = nc.scalar.activation(
                            k_hi[rows, par, c, :, h * TOK:(h + 1) * TOK],
                            src[rows, :].rearrange("p (g t) -> p g t", g=GROUP), ACT.Identity,
                            bias=b_col["k"][rows, c:c + 1])
                    last.then_inc(qk_hi_done[i], 1)

            def slot(s):
                if s.has(-1):
                    for part, cols in enumerate((slice(0, 512), slice(512, 768))):
                        act.wait_ge(pt_done[part], s.at(0))
                        nc.scalar.copy(pt_hi[:, cols], pc_ps[:, cols]).then_inc(pt_hi_done[part], 1)
                if s.has(0):
                    exps(s, 0)
                if s.qk():
                    qk_hi(s, 0)
                    qk_hi(s, 1)
                if s.has(0):
                    exps(s, 1)
                if s.has(-1):
                    act.wait_ge(ctx_done, s.at(0))
                    for h in range(2):
                        rows = slice(HEAD * h, HEAD * (h + 1))
                        last = nc.scalar.copy(ctx_hi[rows], pc3[rows, :, h * TOK:(h + 1) * TOK])
                    last.then_inc(ctx_hi_done, 1)
                if s.has(0):
                    exps(s, 2)
                if s.qk():
                    qk_hi(s, 2)
                if s.has(4):
                    act.wait_ge(xt_done, s.at(5))
                    nc.scalar.copy(xt_hi[:, s.parity(0), :, s.half(0) * TOK:(s.half(0) + 1) * TOK],
                                   a_ps[:, 0:HID].rearrange("p (c t) -> p c t", c=CH)).then_inc(xt_hi_done, 1)
                if s.has(1):
                    act.wait_ge(v_done, s.at(2))
                    nc.scalar.copy(v_hi[:, s.half(1), :], b_ps[:, 0:HID]).then_inc(v_hi_done, 1)

            slots(act, slot, near=range(0, 9))

        @block.vector
        def _(dve):
            pc3 = pc_ps[:, 0:CH * 256].rearrange("p (c n) -> p c n", c=CH)
            k_zero = [t[rows, :, :, :, cols] for t in (k_hi, k_lo)
                      for rows, cols in ((slice(0, 64), slice(TOK, 2 * TOK)), (slice(64, 128), slice(0, TOK)))]
            for t in k_zero:
                for par in range(2):
                    last = nc.vector.memset(t[:, par].rearrange("p c g k -> p (c g) k").bitcast(F32), 0.0)
            last.then_inc(keys_zeroed, 1)
            dve.wait_ge(w_loaded["q"], 16)
            nc.vector.tensor_scalar(stage["q"][:], stage["q"][:], 0.125, None, ALU.mult).then_inc(q_scaled, 1)
            dve.wait_ge(biases_loaded, 64)
            nc.vector.tensor_scalar(b_col["q"][:], b_col["q"][:], 0.125, None, ALU.mult).then_inc(q_scaled, 1)
            nc.vector.memset(bv_rows[:], 1.0).then_inc(ones_made, 1)
            dve.wait_ge(ones_made, 1)
            for c in range(CH):
                nc.vector.tensor_scalar(bv_rows[:, c, :], bv_rows[:, c, :], b_col["v"][:, c:c + 1], None,
                                        ALU.mult).then_inc(bv_repeated, 1)
            for i, w in enumerate("qkvf"):
                dve.wait_ge(w_hi_made, i + 1)
                nc.vector.tensor_tensor(w_lo[w][:], stage[w][:], w_hi[w][:].bitcast(F32),
                                        ALU.subtract).then_inc(w_lo_made, 1)
            dve.wait_ge(bv_projected, 1)
            nc.vector.tensor_tensor(out_bias[:], o_ps[:, 0:HID], bf_row[:], ALU.add).then_inc(out_bias_made, 1)

            def masked_max(s, p):
                for h in (2 * p, 2 * p + 1):
                    cols = slice(h * TOK, (h + 1) * TOK)
                    last = nc.vector.tensor_tensor_reduce(
                        out=neg_scores[:, cols], in0=sc_ps[:, cols], in1=edge_bias[:, s.half(0), :], scale=-1.0,
                        scalar=FLOAT_MAX, op0=ALU.add, op1=ALU.min,
                        accum_out=neg_max[:, s.half(0), h:h + 1])
                last.then_inc(masked[p], 1)

            def qk_lo(s, i):
                par, (w, c) = s.parity(2), QK_CHUNKS[s.j % 2][i]
                src = qk_ps[i][:, 0:GROUP * TOK]
                dve.wait_ge(qk_hi_done[i], s.at(3))
                if w == "q":
                    nc.vector.scalar_tensor_tensor(out=q_lo[:, par, c, :], in0=src, scalar=b_col["q"][:, c:c + 1],
                                                   in1=q_hi[:, par, c, :].bitcast(F32), op0=ALU.add,
                                                   op1=ALU.subtract).then_inc(qk_lo_done[i], 1)
                else:
                    for h in range(2):
                        rows, cols = slice(HEAD * h, HEAD * (h + 1)), slice(h * TOK, (h + 1) * TOK)
                        last = nc.vector.scalar_tensor_tensor(
                            out=k_lo[rows, par, c, :, cols], in0=src[rows, :].rearrange("p (g t) -> p g t", g=GROUP),
                            scalar=b_col["k"][rows, c:c + 1], in1=k_hi[rows, par, c, :, cols].bitcast(F32),
                            op0=ALU.add, op1=ALU.subtract)
                    last.then_inc(qk_lo_done[i], 1)

            def slot(s):
                if s.has(0):
                    dve.wait_ge(edges_done, s.at(1))
                if s.has(-2):
                    h = s.half(0)
                    dve.wait_ge(proj_done, s.at(-1))
                    dve.wait_ge(x_bf_done, s.at(-1))
                    nc.vector.tensor_tensor(resid[:, h, :], o_ps[:, 0:HID], x_bf[:, (s.j - 2) % RING, :],
                                            ALU.add).then_inc(resid_done, 1)
                if s.has(0):
                    long_met(dve, s, keys_zeroed, 1)
                    if s.after(1):
                        dve.wait_ge(exp_done, s.at(0))
                    dve.wait_ge(scores_done[0], s.at(1))
                    masked_max(s, 0)
                    masked_max(s, 1)
                    long_met(dve, s, keys_zeroed, 1)
                    dve.wait_ge(scores_done[1], s.at(1))
                    masked_max(s, 2)
                if s.has(-1):
                    for part, cols in enumerate((slice(0, 512), slice(512, 768))):
                        dve.wait_ge(pt_hi_done[part], s.at(0))
                        nc.vector.tensor_tensor(pt_lo[:, cols], pc_ps[:, cols], pt_hi[:, cols].bitcast(F32),
                                                ALU.subtract).then_inc(pt_lo_done[part], 1)
                if s.has(-2):
                    h = s.half(0)
                    dve.wait_ge(resid_done, s.at(-1))
                    nc.vector.bn_stats(stats[:], resid[:, h, :]).then_inc(stats_done, 1)
                if s.qk():
                    qk_lo(s, 0)
                if s.has(-2):
                    long_met(dve, s, keys_zeroed, 1)
                    dve.wait_ge(stats_done, s.at(-1))
                    nc.vector.bn_aggr(mean_var[:, h, :], stats[:]).then_inc(mean_done, 1)
                if s.qk():
                    qk_lo(s, 1)
                if s.has(-2):
                    dve.wait_ge(rstd_done, s.at(-1))
                    if s.after(4):
                        dve.wait_ge(stored[h], s.turn(-4, 2))
                    nc.vector.tensor_scalar(normed[:, h, :], resid[:, h, :], mean_var[:, h, 0:1], rstd[:, h:h + 1],
                                            ALU.subtract, ALU.mult).then_inc(normed_done, 1)
                if s.has(-1):
                    dve.wait_ge(ctx_hi_done, s.at(0))
                    for h in range(2):
                        rows = slice(HEAD * h, HEAD * (h + 1))
                        last = nc.vector.tensor_tensor(ctx_lo[rows], pc3[rows, :, h * TOK:(h + 1) * TOK],
                                                       ctx_hi[rows].bitcast(F32), ALU.subtract)
                    last.then_inc(ctx_lo_done, 1)
                if s.has(0):
                    dve.wait_ge(exp_done, s.at(1))
                    nc.vector.reciprocal(prob_inv[:, s.half(0), :], prob_sum[:, s.half(0), :]).then_inc(inv_done, 1)
                if s.qk():
                    qk_lo(s, 2)
                if s.has(4):
                    dve.wait_ge(xt_hi_done, s.at(5))
                    cols = slice(s.half(0) * TOK, (s.half(0) + 1) * TOK)
                    nc.vector.tensor_tensor(xt_lo[:, s.parity(0), :, cols],
                                            a_ps[:, 0:HID].rearrange("p (c t) -> p c t", c=CH),
                                            xt_hi[:, s.parity(0), :, cols].bitcast(F32),
                                            ALU.subtract).then_inc(xt_lo_done, 1)
                if s.has(1):
                    dve.wait_ge(v_hi_done, s.at(2))
                    nc.vector.tensor_tensor(v_lo[:, s.half(1), :], b_ps[:, 0:HID],
                                            v_hi[:, s.half(1), :].bitcast(F32), ALU.subtract).then_inc(v_lo_done, 1)

            slots(dve, slot, near=range(-1, 9), turns=((2, -2), (2, -1)))

        @block.tensor
        def _(pe):
            def product(out_ps, pairs):
                for i, (s_hi, s_lo, m_hi, m_lo) in enumerate(pairs):
                    nc.tensor.matmul(out_ps, s_hi, m_hi, start=(i == 0), stop=False)
                    nc.tensor.matmul(out_ps, s_lo, m_hi, start=False, stop=False)
                    last = nc.tensor.matmul(out_ps, s_hi, m_lo, start=False, stop=(i == len(pairs) - 1))
                return last

            def scores(s):
                par = s.parity(0)
                here = slice(s.half(0) * TOK, (s.half(0) + 1) * TOK)
                pe.wait_ge(qk_lo_done[CH - 1], s.at(2 if s.j % 2 == 0 else 1))
                if s.after(1):
                    pe.wait_ge(masked[CH - 1], s.at(0))
                for p in range(CH):
                    last = product(sc_ps[:, p * 256:(p + 1) * 256],
                                   [(q_hi[:, par, p, here], q_lo[:, par, p, here],
                                     k_hi[:, par, p, s.half(0), :], k_lo[:, par, p, s.half(0), :])])
                    if p >= 1:
                        last.then_inc(scores_done[p - 1], 1)

            def transposed_probs(s):
                pe.wait_ge(probs_done, s.at(0))
                if s.after(2):
                    pe.wait_ge(ctx_lo_done, s.at(-1))
                for h in range(HEADS):
                    cols = slice(h * TOK, (h + 1) * TOK)
                    last = nc.tensor.transpose(pc_ps[:, cols], probs[:, s.half(1), cols], ident[:])
                    if h in (3, HEADS - 1):
                        last.then_inc(pt_done[h // 4], 1)

            def qk_products(s, i):
                par, (w, c) = s.parity(2), QK_CHUNKS[s.j % 2][i]
                cols = slice(c * 128, (c + 1) * 128)
                if i == 0:
                    if s.has(3):
                        pe.wait_ge(xt_lo_done, s.at(4))
                    else:
                        pe.wait_ge(qk_lo_done[0], s.at(2))
                elif i == 1 and s.after(0):
                    pe.wait_ge(v_lo_done, s.at(1))
                elif s.after(-1):
                    pe.wait_ge(qk_lo_done[i], s.at(2))
                product(qk_ps[i][:, 0:GROUP * TOK],
                        [(w_hi[w][:, ci, cols], w_lo[w][:, ci, cols], xt_hi[:, par, ci, :], xt_lo[:, par, ci, :])
                         for ci in range(CH)]).then_inc(qk_done[i], 1)

            def context(s):
                v = s.half(1)
                pe.wait_ge(pt_lo_done[0], s.at(0))
                pe.wait_ge(pt_lo_done[1], s.at(0))
                pe.wait_ge(v_lo_done, s.at(0))
                for p in range(CH):
                    two = slice(p * 128, (p + 1) * 128)
                    moving = slice(p * 256, (p + 1) * 256)
                    last = product(pc_ps[:, moving],
                                   [(v_hi[:, v, two], v_lo[:, v, two], pt_hi[:, moving], pt_lo[:, moving])])
                last.then_inc(ctx_done, 1)

            def projection(s):
                pe.wait_ge(ctx_lo_done, s.at(0))
                if s.after(2):
                    pe.wait_ge(resid_done, s.at(-1))
                product(o_ps[:, 0:HID], [(ctx_hi[:, c, :], ctx_lo[:, c, :], w_hi["f"][:, c, :], w_lo["f"][:, c, :])
                                         for c in range(CH)]).then_inc(proj_done, 1)

            def transposed_x(s):
                pe.wait_ge(x_loaded[s.j], s.turn(4, RING))
                if s.qk():
                    pe.wait_ge(qk_lo_done[0], s.at(3))
                elif s.after(-3):
                    pe.wait_ge(xt_lo_done, s.at(4))
                for c in range(CH):
                    cols = slice(c * 128, (c + 1) * 128)
                    last = nc.tensor.transpose(a_ps[:, cols], x_in[:, s.j, cols], ident[:])
                last.then_inc(xt_done, 1)

            def values(s):
                here = slice(s.half(1) * TOK, (s.half(1) + 1) * TOK)
                par = s.parity(1)
                if s.qk():
                    pe.wait_ge(qk_lo_done[1], s.at(3))
                else:
                    pe.wait_ge(v_lo_done, s.at(1))
                product(b_ps[:, 0:HID], [(xt_hi[:, par, c, here], xt_lo[:, par, c, here], w_hi["v"][:, c, :],
                                          w_lo["v"][:, c, :]) for c in range(CH)]).then_inc(v_done, 1)

            pe.wait_ge(ident_made, 1)
            pe.wait_ge(keys_zeroed, 1)
            pe.wait_ge(bv_repeated, CH)
            pe.wait_ge(w_loaded["f"], 16)
            for c in range(CH):
                last = nc.tensor.matmul(o_ps[:, 0:HID], bv_rows[:, c, :], stage["f"][:, c, :], start=(c == 0),
                                        stop=(c == CH - 1))
            last.then_inc(bv_projected, 1)
            pe.wait_ge(out_bias_made, 1)
            pe.wait_ge(w_lo_made, 4)

            def slot(s):
                if s.has(0):
                    scores(s)
                if s.has(-1):
                    transposed_probs(s)
                if s.qk():
                    qk_products(s, 0)
                    qk_products(s, 1)
                if s.has(-1):
                    context(s)
                if s.qk():
                    qk_products(s, 2)
                if s.has(4):
                    transposed_x(s)
                if s.has(1):
                    values(s)
                if s.has(-1):
                    projection(s)

            slots(pe, slot, near=range(-1, 8), turns=((RING, 1),))


_INS = ["x", "adj"] + [f"L0_gnn_{n}" for n in ("Wq", "bq", "Wk", "bk", "Wv", "bv", "Wf", "bf")]


def kernel(**inputs):
    import numpy as _np
    import concourse.bacc as _bacc
    from concourse import mybir as _mybir
    from concourse.bass_utils import run_bass_kernel_spmd as _run

    nc = _bacc.Bacc("TRN2", target_bir_lowering=False, num_devices=1)
    arrays, args = {}, []
    for name in _INS:
        a = _np.ascontiguousarray(inputs[name])
        arrays[f"in_{name}_dram"] = a
        args.append(nc.dram_tensor(f"in_{name}_dram", a.shape, _mybir.dt.from_np(a.dtype), kind="ExternalInput").ap())
    args.append(nc.dram_tensor("out_dram", (GRAPHS, TOK, HID), F32, kind="ExternalOutput").ap())
    build(nc, *args)
    r = _run(nc, [arrays], core_ids=[0])
    return r.results[0]["out_dram"]
```
